# Optimizing a Trainium2 kernel written in Bass

```python
import numpy as np
import jax
import jax.numpy as jnp

def _softmax(x, axis=-1):
    return jax.nn.softmax(x, axis=axis)

def _gelu(x):
    return jax.nn.gelu(x, approximate=True)

def _silu(x):
    return jax.nn.silu(x)

def _sigmoid(x):
    return jax.nn.sigmoid(x)

def _layernorm(x, axis=-1, eps=1e-05):
    m = jnp.mean(x, axis=axis, keepdims=True)
    v = jnp.var(x, axis=axis, keepdims=True)
    return (x - m) / jnp.sqrt(v + eps)

def _scatter_add(tgt, idx, src, axis=0):
    return tgt.at[idx].add(src)

def _segment_sum(src, seg, n):
    return jax.ops.segment_sum(src, seg, n)
kernel_name = 'mk_rec_standalone_d1_rec_r8_da559a'

def setup_inputs(seed: int=0):
    np.random.seed(seed)
    _w = jnp.asarray

    def _rec_inputs():
        import jax
        import jax.numpy as jnp
        _rk = jax.random.key(seed)
        r_target_item = -9.80646e-05 + 1.00041 * jax.random.normal(jax.random.fold_in(_rk, 1), (2048, 128), jnp.float32)
        r_history_sequence = -9.97791e-05 + 0.999858 * jax.random.normal(jax.random.fold_in(_rk, 2), (2048, 200, 128), jnp.float32)
        r_mask = jax.random.randint(jax.random.fold_in(_rk, 3), (2048, 200), 0, 2, jnp.int32)
        return (r_target_item, r_history_sequence, r_mask)
    r_target_item, r_history_sequence, r_mask = _rec_inputs()

    def _L0_rec_setup():
        import jax, jax.numpy as jnp
        import numpy as np
        NUM_HEADS = 4
        HEAD_DIM = 32
        SCALE = HEAD_DIM ** 0.5
        key = jax.random.key(seed)
        ks = jax.random.split(key, 7)
        B, L, D = (512, 200, 128)
        return {'target_item': jax.random.normal(ks[0], (B, D), dtype=jnp.float32), 'history_sequence': jax.random.normal(ks[1], (B, L, D), dtype=jnp.float32), 'mask': jax.random.randint(ks[2], (B, L), 0, 2, dtype=jnp.int32), 'W_q': jax.random.normal(ks[3], (D, D), dtype=jnp.float32) * 0.05, 'W_k': jax.random.normal(ks[4], (D, D), dtype=jnp.float32) * 0.05, 'W_v': jax.random.normal(ks[5], (D, D), dtype=jnp.float32) * 0.05, 'W_o': jax.random.normal(ks[6], (D, D), dtype=jnp.float32) * 0.05}
    _L0_rec_all = _L0_rec_setup()
    _L0_rec_in = {k: v for k, v in _L0_rec_all.items() if k in ('W_q', 'W_k', 'W_v', 'W_o')}
    del _L0_rec_all
    return {'r_target_item': r_target_item, 'r_history_sequence': r_history_sequence, 'r_mask': r_mask, 'L0_rec_W_q': _L0_rec_in['W_q'], 'L0_rec_W_k': _L0_rec_in['W_k'], 'L0_rec_W_v': _L0_rec_in['W_v'], 'L0_rec_W_o': _L0_rec_in['W_o']}

def reference(r_target_item, r_history_sequence, r_mask, L0_rec_W_q, L0_rec_W_k, L0_rec_W_v, L0_rec_W_o):
    import jax
    import jax.numpy as jnp

    def _L0_rec_ref(target_item, history_sequence, mask, W_q, W_k, W_v, W_o):
        import jax, jax.numpy as jnp
        import numpy as np
        NUM_HEADS = 4
        HEAD_DIM = 32
        SCALE = HEAD_DIM ** 0.5
        B = target_item.shape[0]
        q = target_item @ W_q.T
        k = history_sequence @ W_k.T
        v = history_sequence @ W_v.T
        q = q.reshape(B, NUM_HEADS, HEAD_DIM)
        k = k.reshape(B, -1, NUM_HEADS, HEAD_DIM).transpose(0, 2, 1, 3)
        v = v.reshape(B, -1, NUM_HEADS, HEAD_DIM).transpose(0, 2, 1, 3)
        scores = jnp.einsum('bhd,bhld->bhl', q, k) / SCALE
        m = (mask != 0)[:, None, :]
        scores = jnp.where(m, scores, -jnp.inf)
        attn = jax.nn.softmax(scores, axis=-1)
        out = jnp.einsum('bhl,bhld->bhd', attn, v)
        out = out.reshape(B, NUM_HEADS * HEAD_DIM)
        return out @ W_o.T
    y = _L0_rec_ref(r_target_item, r_history_sequence, r_mask, L0_rec_W_q, L0_rec_W_k, L0_rec_W_v, L0_rec_W_o)
    return y

_drawn_inputs = setup_inputs


def setup_inputs(seed=0):
    import zlib

    import numpy as np

    out = dict(_drawn_inputs(seed))
    spreads = {}
    factors = {}
    for name, (base, spread) in spreads.items():
        noise = np.random.default_rng([zlib.crc32(name.encode()), seed]).standard_normal(out[name].shape)
        drawn = base * np.exp(spread * noise) if base else spread * noise
        out[name] = jnp.asarray(drawn.astype(out[name].dtype))
    for name, factor in factors.items():
        out[name] = (out[name] * factor).astype(out[name].dtype)
    return out
```

```python
from contextlib import ExitStack

import concourse.bass as bass
from concourse import mybir


def target_attention(nc, target, history, mask, w_q, w_k, w_v, w_o, y):
    F32 = mybir.dt.float32
    BF16 = mybir.dt.bfloat16
    I32 = mybir.dt.int32
    ALU = mybir.AluOpType
    ACT = mybir.ActivationFunctionType
    AX = mybir.AxisListType

    B, D = target.shape
    L = mask.shape[1]
    P = 128
    HD = 32
    H = D // HD
    NB = D // HD
    A = P // HD
    SEG = 8
    ROWS = L // SEG
    T = (ROWS + 1) // 2
    JJ = 2 * SEG
    SUB = 2
    GB = SUB * P // JJ
    G = 2
    R = P // (G * GB)
    CG = R * G
    CHUNKS = B // P
    PAIRS = CHUNKS * R
    Q = 2 * SUB
    S = T * JJ
    TP = (T + 1) // 2
    SP = TP * HD
    SPREAD = TP * 2 * H
    NEG = -3.0e38
    FLOOR = -1.0e37
    SCALE = HD ** 0.5
    assert CG * GB == P and PAIRS * G * GB == B and GB == 2 * P // JJ

    hist = history.rearrange("b l d -> (b l) d").rearrange("(n u s r) d -> n s u (r d)", u=SUB, s=P // 2, r=ROWS)

    ctx = ExitStack()
    with ctx:
        def sb(name, shape, dt=F32):
            return ctx.enter_context(nc.sbuf_tensor(name, shape, dt))

        def bank(name, width=512):
            return ctx.enter_context(nc.psum_tensor(name, [P, width], F32))

        def sem(name):
            return ctx.enter_context(nc.semaphore(name))

        x = [sb(f"x{k}", [P, SUB, T * D]) for k in range(CG)]
        xT = [[sb(f"xT{k}{g}", [P, SUB, T, NB, HD]) for g in range(G)] for k in range(2)]
        keys = [sb(f"keys{r}", [P, G * SUB, 2, NB, HD]) for r in range(R)]
        uT = sb("uT", [P, NB * H, CG, SUB, 2])
        probs = [sb(f"probs{g}", [P, SP]) for g in range(G)]
        probsT = [sb(f"probsT{g}", [P, TP, 2, A, H]) for g in range(G)]
        weights = [sb(f"weights{g}", [P, SUB, 2, TP, HD]) for g in range(G)]
        rowmax = sb("rowmax", [P, G])
        bias = sb("bias", [P, G])
        total = sb("total", [P, G])
        reciprocal = sb("reciprocal", [P, G])
        inverse = sb("inverse", [P, G])
        used_rows = sb("used_rows", [P, 3])
        mask_in = sb("mask_in", [P, L], I32)
        maskbias = sb("maskbias", [P, T, SEG, 2], BF16)
        picks = sb("picks", [P, CG, SUB, 2, 2, A, H], BF16)
        ident = sb("ident", [P, P])
        spreads = sb("spreads", [P, SUB, 2, 2, JJ])
        tgt = sb("tgt", [P, D])
        tgtT = sb("tgtT", [P, A, CG, SUB, 2])
        ctx_rows = sb("ctx_rows", [P, D])
        ctxT = sb("ctxT", [P, H, P])
        y_out = sb("y_out", [P, D])
        scoreW = sb("scoreW", [P, H * D])
        outW = sb("outW", [P, H * D])
        wq = sb("wq", [P, D])
        wk = sb("wk", [P, D])
        wv = sb("wv", [P, D])
        wo = sb("wo", [P, D])
        woT = sb("woT", [P, D])
        wq_heads = sb("wq_heads", [P, H, D])
        wv_heads = sb("wv_heads", [P, H, D])

        ps_scores = [bank(f"ps_scores{g}") for g in range(G)]
        ps_spread = [bank(f"ps_spread{g}") for g in range(G)]
        ps_ctx = bank("ps_ctx")
        ps_ctxT = bank("ps_ctxT")
        ps_u = bank("ps_u")
        ps_misc = bank("ps_misc")

        x_loaded = [sem(f"x_loaded{k}") for k in range(CG)]
        xT_ready = sem("xT_ready")
        scores_ready = sem("scores_ready")
        rowmax_ready = sem("rowmax_ready")
        bias_ready = sem("bias_ready")
        exp_ready = sem("exp_ready")
        reciprocal_ready = sem("reciprocal_ready")
        inverse_ready = sem("inverse_ready")
        probs_ready = sem("probs_ready")
        probsT_ready = sem("probsT_ready")
        spread_ready = sem("spread_ready")
        weights_ready = sem("weights_ready")
        ctx_ready = sem("ctx_ready")
        ctx_copied = sem("ctx_copied")
        ctxT_ready = sem("ctxT_ready")
        ctxT_copied = sem("ctxT_copied")
        keys_ready = sem("keys_ready")
        tgt_loaded = sem("tgt_loaded")
        tgtT_ready = sem("tgtT_ready")
        tgtT_copied = sem("tgtT_copied")
        u_ready = sem("u_ready")
        uT_ready = sem("uT_ready")
        mask_loaded = sem("mask_loaded")
        maskbias_ready = sem("maskbias_ready")
        y_ready = sem("y_ready")
        y_copied = sem("y_copied")
        y_stored = sem("y_stored")
        y_free = sem("y_free")
        w_loaded = sem("w_loaded")
        zeroed_dve = sem("zeroed_dve")
        zeroed_pool = sem("zeroed_pool")
        zeroed_act = sem("zeroed_act")
        consts_ready = sem("consts_ready")
        heads_ready = sem("heads_ready")
        woT_ready = sem("woT_ready")
        woT_copied = sem("woT_copied")
        products_ready = sem("products_ready")
        products_copied = sem("products_copied")

        ZEROED = 3 + 2 * G

        def groups(c, r, g):
            return c * CG + (G * r + g + 1)

        def pairs(c, r):
            return c * R + (r + 1)

        block = ctx.enter_context(nc.Block())

        @block.sync
        def _(sp):
            def load(c, k, first):
                if not first:
                    sp.wait_ge(ctx_ready, c * R + (k // G - R + 1))
                src = hist[c * CG + k]
                sp.dma_start(x[k][0:P:2, :, :], src[:, :, 0:T * D]).then_inc(x_loaded[k], 16)
                sp.dma_start(x[k][1:P:2, :, D:T * D], src[:, :, T * D:ROWS * D]).then_inc(x_loaded[k], 16)

            sp.wait_ge(zeroed_dve, 1)
            for k in range(CG):
                load(0, k, True)
                if k == 0:
                    sp.dma_start(wq[:], w_q).then_inc(w_loaded, 16)
                    sp.dma_start(wk[:], w_k).then_inc(w_loaded, 16)
                    sp.dma_start(wv[:], w_v).then_inc(w_loaded, 16)
                    sp.dma_start(wo[:], w_o).then_inc(w_loaded, 16)
            with sp.Fori(1, CHUNKS) as c:
                for k in range(CG):
                    load(c, k, False)

        @block.gpsimd
        def _(pool):
            def load_target(c):
                pool.dma_start(tgt[:], target.rearrange("(c p) d -> c p d", p=P)[c]).then_inc(tgt_loaded, 16)

            def load_mask(c):
                pool.dma_start(mask_in[:], mask.rearrange("(c p) l -> c p l", p=P)[c]).then_inc(mask_loaded, 16)

            def store_y(c):
                pool.wait_ge(y_copied, c + 1)
                pool.dma_start(y.rearrange("(c p) d -> c p d", p=P)[c], y_out[:]).then_inc(y_stored, 16)
                pool.wait_ge(y_stored, 16 * c + 16)
                pool.sem_inc(y_free, 1)

            load_target(0)
            load_mask(0)
            pool.sem_inc(y_free, 1)
            nc.gpsimd.memset(ident[:], 0.0).then_inc(zeroed_pool, 1)
            nc.gpsimd.memset(picks[:], 0.0).then_inc(zeroed_pool, 1)
            for r in range(R):
                nc.gpsimd.memset(keys[r][:], 0.0).then_inc(zeroed_pool, 1)
            nc.gpsimd.memset(maskbias[:, 0, :, 1], NEG).then_inc(zeroed_pool, 1)
            pool.wait_ge(zeroed_pool, R + 3)
            nc.gpsimd.affine_select(out=ident[:], in_=ident[:], compare_op=ALU.not_equal, fill=1.0, base=0,
                                    pattern=[[-1, P]], channel_multiplier=1).then_inc(consts_ready, 1)
            for b2 in range(2):
                view = picks[:, :, :, b2, b2, :, :].rearrange("p g s a h -> p (g s) a h")
                nc.gpsimd.affine_select(out=view, in_=view, compare_op=ALU.not_equal, fill=1.0, base=-b2,
                                        pattern=[[-8, CG * SUB], [-2, A], [0, H]],
                                        channel_multiplier=1).then_inc(consts_ready, 1)

            def chunk(c, first, last):
                if not last:
                    pool.wait_ge(u_ready, c + 1)
                    load_target(c + 1)
                    pool.wait_ge(maskbias_ready, c + 1)
                    load_mask(c + 1)
                if not first:
                    store_y(c - 1)

            chunk(0, True, False)
            with pool.Fori(1, CHUNKS - 1) as c:
                chunk(c, False, False)
            chunk(CHUNKS - 1, False, True)
            store_y(CHUNKS - 1)
            pool.wait_ge(y_stored, 16 * CHUNKS)

        @block.vector
        def _(dve):
            def transpose_rows(c, r, g, sub, part, first):
                t0, t1 = (0, T // 2 + 1) if part == 0 else (T // 2 + 1, T)
                k = G * r + g
                if sub == 0 and part == 0:
                    dve.wait_ge(x_loaded[k], c * 32 + 32)
                    if not (first and r < 2):
                        dve.wait_ge(scores_ready, groups(c, r - 2, g))
                op = nc.vector.transpose(xT[r % 2][g][:, sub, t0:t1, :, :].rearrange("p t b j -> p (t b j)"),
                                         x[k][:, sub, t0 * D:t1 * D])
                if sub == SUB - 1 and part == 1:
                    op.then_inc(xT_ready, 1)

            def row_bias(c, r, g):
                dve.wait_ge(scores_ready, groups(c, r, g))
                nc.vector.reduce_max(rowmax[:, g:g + 1], ps_scores[g][:, 0:S], AX.X).then_inc(rowmax_ready, 1)
                dve.wait_ge(rowmax_ready, groups(c, r, g))
                nc.vector.tensor_scalar(bias[:, g:g + 1], rowmax[:, g:g + 1], FLOOR, -1.0 / SCALE, ALU.max,
                                        ALU.mult).then_inc(bias_ready, 1)

            def invert(c, r, g):
                dve.wait_ge(exp_ready, groups(c, r, g))
                nc.vector.reciprocal(reciprocal[:, g:g + 1], total[:, g:g + 1]).then_inc(reciprocal_ready, 1)
                dve.wait_ge(reciprocal_ready, groups(c, r, g))
                nc.vector.tensor_tensor(inverse[:, g:g + 1], reciprocal[:, g:g + 1], used_rows[:, 2:3],
                                        ALU.mult).then_inc(inverse_ready, 1)

            def transpose_probs(c, r, g, first):
                dve.wait_ge(probs_ready, groups(c, r, g))
                if not (first and r < 1):
                    dve.wait_ge(spread_ready, groups(c, r - 1, g))
                nc.vector.transpose(probsT[g][:].rearrange("p t b a h -> p (t b a h)"),
                                    probs[g][:]).then_inc(probsT_ready, 1)

            def make_maskbias(c):
                dve.wait_ge(mask_loaded, 16 * c + 16)
                for half in range(2):
                    src = mask_in[:].rearrange("p (s r) -> p r s", s=SEG)[:, half * T:T + half * (T - 1), :]
                    last = nc.vector.tensor_scalar(maskbias[:, half:T, :, half], src, 0.0, NEG, ALU.is_equal,
                                                   ALU.mult)
                last.then_inc(maskbias_ready, 1)

            for k in range(CG):
                last = nc.vector.memset(x[k][:, :, 0:D], 0.0)
            last.then_inc(zeroed_dve, 1)
            for g in range(G):
                nc.vector.memset(probs[g][:, S:SP], 0.0).then_inc(zeroed_dve, 1)
                nc.vector.memset(weights[g][:], 0.0).then_inc(zeroed_dve, 1)
            nc.vector.memset(wq_heads[:], 0.0).then_inc(zeroed_dve, 1)
            nc.vector.memset(wv_heads[:], 0.0).then_inc(zeroed_dve, 1)
            dve.wait_ge(consts_ready, 1)
            for sub in range(SUB):
                nc.vector.tensor_copy(spreads[:, sub], ident[:, 64 * sub:64 * sub + 64].rearrange(
                    "p (b t j) -> p t b j", b=2, t=2)).then_inc(zeroed_dve, 1)
            cols = ident[:].rearrange("p (s c) -> p s c", s=SUB)
            for b2 in range(2):
                nc.vector.reduce_sum(used_rows[:, b2:b2 + 1], cols[:, :, 48 * b2:48 * b2 + 16],
                                     AX.XY).then_inc(zeroed_dve, 1)
            dve.wait_ge(zeroed_dve, ZEROED + 4)
            nc.vector.tensor_tensor(used_rows[:, 2:3], used_rows[:, 0:1], used_rows[:, 1:2],
                                    ALU.add).then_inc(zeroed_dve, 1)
            dve.wait_ge(zeroed_pool, R + 3)
            make_maskbias(0)
            dve.wait_ge(u_ready, 1)
            nc.vector.transpose(uT[:].rearrange("p n g s b -> p (n g s b)"), ps_u[:]).then_inc(uT_ready, 1)
            dve.wait_ge(zeroed_dve, ZEROED + 5)
            for g in range(G):
                for sub in range(SUB):
                    for part in range(2):
                        transpose_rows(0, 0, g, sub, part, True)

            def chunk(c, first, last):
                for r in range(R):
                    ahead = not (last and r == R - 1)
                    c1, r1 = (c, r + 1) if r + 1 < R else (c + 1, 0)

                    def rows(g, sub, part):
                        if ahead:
                            transpose_rows(c1, r1, g, sub, part, first and r + 1 < R)

                    rows(0, 0, 0)
                    rows(0, 0, 1)
                    row_bias(c, r, 0)
                    rows(0, 1, 0)
                    invert(c, r, 0)
                    rows(0, 1, 1)
                    transpose_probs(c, r, 0, first)
                    rows(1, 0, 0)
                    row_bias(c, r, 1)
                    rows(1, 0, 1)
                    invert(c, r, 1)
                    rows(1, 1, 0)
                    transpose_probs(c, r, 1, first)
                    if r == R - 1 and not last:
                        make_maskbias(c + 1)
                    rows(1, 1, 1)
                    if r == 1 and not last:
                        dve.wait_ge(u_ready, c + 2)
                        dve.wait_ge(keys_ready, pairs(c, R - 1))
                        nc.vector.transpose(uT[:].rearrange("p n g s b -> p (n g s b)"),
                                            ps_u[:]).then_inc(uT_ready, 1)

            chunk(0, True, False)
            with dve.Fori(1, CHUNKS - 1) as c:
                chunk(c, False, False)
            chunk(CHUNKS - 1, False, True)

        @block.scalar
        def _(act):
            def copy_ctx(c, r, first):
                act.wait_ge(ctx_ready, pairs(c, r))
                if not (first and r < 1):
                    act.wait_ge(ctxT_ready, pairs(c, r - 1))
                nc.scalar.copy(ctx_rows[:], ps_ctx[:, 0:D]).then_inc(ctx_copied, 1)

            def copy_ctxT(c, r, first):
                act.wait_ge(ctxT_ready, pairs(c, r))
                if r % R == 0 and not (first and r == 0):
                    act.wait_ge(y_ready, c + r // R)
                n = (r % R) * G * GB
                nc.scalar.copy(ctxT[:, :, n:n + G * GB],
                               ps_ctxT[:, 0:P].rearrange("p (n h) -> p h n", h=H)).then_inc(ctxT_copied, 1)

            def place_weights(c, r, g):
                act.wait_ge(spread_ready, groups(c, r, g))
                for a in range(A):
                    rows = slice(HD * a, HD * a + HD)
                    dst = weights[g][rows, :, :, :, 2 * H * a:2 * H * a + 2 * H].rearrange("p s u t m -> p (s u t) m")
                    src = ps_spread[g][rows, 0:SUB * 2 * SPREAD].rearrange("p (n m) -> p n m", m=2 * H)
                    last = nc.scalar.copy(dst, src)
                last.then_inc(weights_ready, 1)

            def exponential(c, r, g, first):
                act.wait_ge(bias_ready, groups(c, r, g))
                if not (first and r < 1):
                    act.wait_ge(probsT_ready, groups(c, r - 1, g))
                nc.scalar.activation(probs[g][:, 0:S], ps_scores[g][:, 0:S], ACT.Exp, bias=bias[:, g:g + 1],
                                     scale=1.0 / SCALE, accum_out=total[:, g:g + 1]).then_inc(exp_ready, 1)

            def normalize(c, r, g):
                act.wait_ge(inverse_ready, groups(c, r, g))
                nc.scalar.activation(probs[g][:, 0:S], probs[g][:, 0:S], ACT.Copy,
                                     scale=inverse[:, g:g + 1]).then_inc(probs_ready, 1)

            def copy_targetT(c, first):
                act.wait_ge(tgtT_ready, c + 1)
                if not first:
                    act.wait_ge(u_ready, c)
                nc.scalar.copy(tgtT[:].rearrange("p a g s b -> p a (g s) b"),
                               ps_misc[:, 0:P].rearrange("p (n a b) -> p a n b", a=A, b=2)).then_inc(tgtT_copied, 1)

            def copy_y(c):
                act.wait_ge(y_ready, c + 1)
                act.wait_ge(y_free, c + 1)
                nc.scalar.copy(y_out[:], ps_misc[:, 0:D]).then_inc(y_copied, 1)

            def make_keys(c, r):
                act.wait_ge(uT_ready, c + 1)
                for a in range(A):
                    rows = slice(HD * a, HD * a + HD)
                    for b2 in range(2):
                        dst = keys[r][rows, :, b2, :, 16 * b2 + H * a:16 * b2 + H * a + H]
                        src = uT[rows, :, G * r:G * r + G, :, b2].rearrange("p (h b) g s -> p (g s) b h", h=H)
                        last = nc.scalar.copy(dst, src)
                last.then_inc(keys_ready, 1)

            act.wait_ge(w_loaded, 64)
            act.wait_ge(zeroed_dve, ZEROED)
            for h in range(H):
                rows = slice(HD * h, HD * h + HD)
                nc.scalar.copy(wq_heads[rows, h, :], wq[rows, :])
                last = nc.scalar.copy(wv_heads[rows, h, :], wv[rows, :])
            last.then_inc(heads_ready, 1)
            act.wait_ge(woT_ready, 1)
            nc.scalar.copy(woT[:], ps_ctxT[:, 0:P]).then_inc(woT_copied, 1)
            copy_targetT(0, True)
            act.wait_ge(products_ready, 1)
            nc.scalar.copy(scoreW[:], ps_u[:]).then_inc(products_copied, 1)
            act.wait_ge(products_ready, 2)
            nc.scalar.copy(outW[:], ps_ctx[:]).then_inc(products_copied, 1)
            act.wait_ge(zeroed_pool, R + 3)
            for r in range(R - 1):
                make_keys(0, r)

            def chunk(c, first, last):
                for r in range(R):
                    if not (first and r < 2):
                        copy_ctx(c, r - 2, first)
                    if not (first and r < 1):
                        for g in range(G):
                            place_weights(c, r - 1, g)
                    if r == 0 and not last:
                        copy_targetT(c + 1, False)
                    if r == 2 and not first:
                        copy_y(c - 1)
                    if not (first and r < 2):
                        copy_ctxT(c, r - 2, first)
                    for g in range(G):
                        exponential(c, r, g, first)
                        normalize(c, r, g)
                    if r == 0:
                        make_keys(c, R - 1)
                    elif r == 2 and not last:
                        make_keys(c + 1, 0)
                        make_keys(c + 1, 1)
                    elif r == 3 and not last:
                        make_keys(c + 1, 2)

            chunk(0, True, False)
            with act.Fori(1, CHUNKS - 1) as c:
                chunk(c, False, False)
            chunk(CHUNKS - 1, False, True)
            copy_ctx(CHUNKS - 1, R - 2, False)
            for g in range(G):
                place_weights(CHUNKS - 1, R - 1, g)
            copy_ctxT(CHUNKS - 1, R - 2, False)
            copy_ctx(CHUNKS - 1, R - 1, False)
            copy_ctxT(CHUNKS - 1, R - 1, False)
            copy_y(CHUNKS - 1)

        @block.tensor
        def _(pe):
            def scores(c, r, g, first):
                pe.wait_ge(xT_ready, groups(c, r, g))
                if g == 0:
                    pe.wait_ge(keys_ready, pairs(c, r))
                if g == 0 and r == 0:
                    pe.wait_ge(maskbias_ready, c + 1)
                if not (first and r < 1):
                    pe.wait_ge(exp_ready, groups(c, r - 1, g))
                for q in range(Q):
                    sub, b2 = q // 2, q % 2
                    nc.tensor.matmul(ps_scores[g][HD * q:HD * q + HD, 0:S],
                                     picks[:, G * r + g, sub, b2, :, :, :].rearrange("p b a h -> p (b a h)"),
                                     maskbias[:].rearrange("p t s f -> p (t s f)"),
                                     start=True, stop=False, tile_position=(0, HD * q))
                for b in range(NB):
                    for q in range(Q):
                        sub, b2 = q // 2, q % 2
                        last = nc.tensor.matmul(ps_scores[g][HD * q:HD * q + HD, 0:S],
                                                keys[r][:, SUB * g + sub, b2, b, :],
                                                xT[r % 2][g][:, sub, :, b, JJ * b2:JJ * b2 + JJ],
                                                start=False, stop=(b == NB - 1), tile_position=(0, HD * q))
                last.then_inc(scores_ready, 1)

            def spread(c, r, g, first):
                pe.wait_ge(probsT_ready, groups(c, r, g))
                if not (first and r < 1):
                    pe.wait_ge(weights_ready, groups(c, r - 1, g))
                for n in range(2 * SUB):
                    for a in range(A):
                        last = nc.tensor.matmul(ps_spread[g][HD * a:HD * a + HD, SPREAD * n:SPREAD * n + SPREAD],
                                                spreads[:, n // 2, n % 2, :, :].rearrange("p b j -> p (b j)"), probsT[g][:, :, :, a, :],
                                                start=True, stop=True, tile_position=(0, HD * a))
                last.then_inc(spread_ready, 1)

            def weighted(c, r, first):
                for g in range(G):
                    pe.wait_ge(weights_ready, groups(c, r, g))
                if not (first and r < 1):
                    pe.wait_ge(ctx_copied, pairs(c, r - 1))
                for t in range(T):
                    for g in range(G):
                        for sub in range(SUB):
                            q = SUB * g + sub
                            last = nc.tensor.matmul(ps_ctx[HD * q:HD * q + HD, 0:D],
                                                    weights[g][:, sub, t % 2, t // 2, :],
                                                    x[G * (r % R) + g][:, sub, t * D:t * D + D],
                                                    start=(t == 0), stop=(t == T - 1), tile_position=(0, HD * q))
                last.then_inc(ctx_ready, 1)

            def transpose_ctx(c, r, first):
                pe.wait_ge(ctx_copied, pairs(c, r))
                if not (first and r < 1):
                    pe.wait_ge(ctxT_copied, pairs(c, r - 1))
                nc.tensor.transpose(ps_ctxT[:, 0:P], ctx_rows[:], ident[:]).then_inc(ctxT_ready, 1)

            def transpose_target(c):
                pe.wait_ge(tgt_loaded, 16 * c + 16)
                nc.tensor.transpose(ps_misc[:, 0:P], tgt[:], ident[:]).then_inc(tgtT_ready, 1)

            def score_vectors(c):
                pe.wait_ge(tgtT_copied, c + 1)
                nc.tensor.matmul(ps_u[:], tgtT[:].rearrange("p a g s b -> p (a g s b)"), scoreW[:],
                                 start=True, stop=True).then_inc(u_ready, 1)

            def project(c):
                pe.wait_ge(ctxT_copied, pairs(c, R - 1))
                for h in range(H):
                    last = nc.tensor.matmul(ps_misc[:, 0:D], ctxT[:, h, :], outW[:, h * D:h * D + D],
                                            start=(h == 0), stop=(h == H - 1))
                last.then_inc(y_ready, 1)

            pe.wait_ge(consts_ready, 3)
            pe.wait_ge(zeroed_dve, ZEROED + 5)
            transpose_target(0)
            pe.wait_ge(w_loaded, 64)
            nc.tensor.transpose(ps_ctxT[:, 0:P], wo[:], ident[:]).then_inc(woT_ready, 1)
            pe.wait_ge(heads_ready, 1)
            for h in range(H):
                last = nc.tensor.matmul(ps_u[:, h * D:h * D + D], wq_heads[:, h, :], wk[:], start=True, stop=True)
            last.then_inc(products_ready, 1)
            pe.wait_ge(woT_copied, 1)
            for h in range(H):
                last = nc.tensor.matmul(ps_ctx[:, h * D:h * D + D], wv_heads[:, h, :], woT[:], start=True, stop=True)
            last.then_inc(products_ready, 1)
            pe.wait_ge(products_copied, 2)
            score_vectors(0)

            def chunk(c, first, last):
                for r in range(R):
                    if not (first and r < 1):
                        for g in range(G):
                            spread(c, r - 1, g, first)
                    if r == 0 and not last:
                        transpose_target(c + 1)
                    if r == 1 and not last:
                        pe.wait_ge(uT_ready, c + 1)
                        score_vectors(c + 1)
                    if r == 2 and not first:
                        pe.wait_ge(tgtT_copied, c + 1 if last else c + 2)
                        project(c - 1)
                    if not (first and r < 2):
                        transpose_ctx(c, r - 2, first)
                    for g in range(G):
                        scores(c, r, g, first)
                    if not (first and r < 1):
                        weighted(c, r - 1, first)

            chunk(0, True, False)
            with pe.Fori(1, CHUNKS - 1) as c:
                chunk(c, False, False)
            chunk(CHUNKS - 1, False, True)
            for g in range(G):
                spread(CHUNKS - 1, R - 1, g, False)
            transpose_ctx(CHUNKS - 1, R - 2, False)
            weighted(CHUNKS - 1, R - 1, False)
            transpose_ctx(CHUNKS - 1, R - 1, False)
            pe.wait_ge(y_copied, CHUNKS - 1)
            project(CHUNKS - 1)


_INS = ["r_target_item", "r_history_sequence", "r_mask", "L0_rec_W_q", "L0_rec_W_k", "L0_rec_W_v", "L0_rec_W_o"]


def kernel(**inputs):
    import concourse.bacc as bacc
    import numpy as np
    from concourse.bass_utils import run_bass_kernel_spmd

    nc = bacc.Bacc("TRN2", target_bir_lowering=False, num_devices=1)
    arrays, args = {}, []
    for name in _INS:
        a = np.ascontiguousarray(inputs[name])
        arrays[name] = a
        args.append(nc.dram_tensor(name, a.shape, mybir.dt.from_np(a.dtype), kind="ExternalInput").ap())
    y = nc.dram_tensor("y", inputs["r_target_item"].shape, mybir.dt.float32, kind="ExternalOutput").ap()
    target_attention(nc, *args, y)
    return run_bass_kernel_spmd(nc, [arrays], core_ids=[0]).results[0]["y"]
```

```python
from contextlib import ExitStack

import concourse.bass as bass
from concourse import mybir


def target_attention(nc, target, history, mask, w_q, w_k, w_v, w_o, y):
    F32 = mybir.dt.float32
    BF16 = mybir.dt.bfloat16
    I32 = mybir.dt.int32
    ALU = mybir.AluOpType
    ACT = mybir.ActivationFunctionType
    AX = mybir.AxisListType

    B, D = target.shape
    L = mask.shape[1]
    P = 128
    HD = 32
    H = D // HD
    NB = D // HD
    A = P // HD
    SEG = 8
    ROWS = L // SEG
    T = (ROWS + 1) // 2
    JJ = 2 * SEG
    SUB = 2
    GB = SUB * P // JJ
    G = 2
    R = P // (G * GB)
    CG = R * G
    CHUNKS = B // P
    PAIRS = CHUNKS * R
    Q = 2 * SUB
    S = T * JJ
    TP = (T + 1) // 2
    SP = TP * HD
    SPREAD = G * TP * 2 * H
    NEG = -3.0e38
    FLOOR = -1.0e37
    PEAK = 1.0e30
    SE = S + 1
    SM = S + 2
    SCALE = HD ** 0.5
    assert CG * GB == P and PAIRS * G * GB == B and GB == 2 * P // JJ

    hist = history.rearrange("b l d -> (b l) d").rearrange("(n u s r) d -> n s u (r d)", u=SUB, s=P // 2, r=ROWS)

    ctx = ExitStack()
    with ctx:
        def sb(name, shape, dt=F32):
            return ctx.enter_context(nc.sbuf_tensor(name, shape, dt))

        def bank(name, width=512):
            return ctx.enter_context(nc.psum_tensor(name, [P, width], F32))

        def sem(name):
            return ctx.enter_context(nc.semaphore(name))

        x = [sb(f"x{k}", [P, SUB, T * D]) for k in range(CG)]
        xT = [[sb(f"xT{k}{g}", [P, SUB, T, NB, HD]) for g in range(G)] for k in range(2)]
        keys = [sb(f"keys{r}", [P, G * SUB, 2, NB, HD]) for r in range(R)]
        uT = sb("uT", [P, NB * H, CG, SUB, 2])
        probs = [sb(f"probs{g}", [P, SP]) for g in range(G)]
        probsT = sb("probsT", [P, G, TP, 2, A, H])
        weights = sb("weights", [P, 2, SUB, G, TP, HD])
        bias = sb("bias", [P, G])
        total = sb("total", [P, G])
        inverse = sb("inverse", [P, G])
        used_rows = sb("used_rows", [P, 3])
        mask_in = sb("mask_in", [P, L], I32)
        maskbias = sb("maskbias", [P, T, SEG, 2], BF16)
        picks = sb("picks", [P, CG, SUB, 2, 2, A, H], BF16)
        ident = sb("ident", [P, P])
        spreads = sb("spreads", [P, SUB, 2, 2, JJ])
        tgt = sb("tgt", [P, D])
        tgtT = sb("tgtT", [P, A, CG, SUB, 2])
        ctx_rows = sb("ctx_rows", [P, D])
        ctxT = sb("ctxT", [P, H, P])
        y_out = sb("y_out", [P, D])
        scoreW = sb("scoreW", [P, H * D])
        outW = sb("outW", [P, H * D])
        wq = sb("wq", [P, D])
        wk = sb("wk", [P, D])
        wv = sb("wv", [P, D])
        wo = sb("wo", [P, D])
        woT = sb("woT", [P, D])
        wq_heads = sb("wq_heads", [P, H, D])
        wv_heads = sb("wv_heads", [P, H, D])

        ps_scores = [bank(f"ps_scores{g}") for g in range(G)]
        ps_spread = bank("ps_spread")
        ps_product = bank("ps_product")
        ps_ctx = bank("ps_ctx")
        ps_ctxT = bank("ps_ctxT")
        ps_u = bank("ps_u")
        ps_misc = bank("ps_misc")

        x_loaded = [sem(f"x_loaded{k}") for k in range(CG)]
        xT_ready = sem("xT_ready")
        scores_ready = sem("scores_ready")
        bias_ready = sem("bias_ready")
        exp_ready = sem("exp_ready")
        inverse_ready = sem("inverse_ready")
        probs_ready = sem("probs_ready")
        probsT_ready = sem("probsT_ready")
        spread_ready = sem("spread_ready")
        weights_ready = sem("weights_ready")
        ctx_ready = sem("ctx_ready")
        ctx_copied = sem("ctx_copied")
        ctxT_ready = sem("ctxT_ready")
        ctxT_copied = sem("ctxT_copied")
        keys_ready = sem("keys_ready")
        tgt_loaded = sem("tgt_loaded")
        tgtT_ready = sem("tgtT_ready")
        tgtT_copied = sem("tgtT_copied")
        u_ready = sem("u_ready")
        uT_ready = sem("uT_ready")
        mask_loaded = sem("mask_loaded")
        maskbias_ready = sem("maskbias_ready")
        y_ready = sem("y_ready")
        y_copied = sem("y_copied")
        y_stored = sem("y_stored")
        y_free = sem("y_free")
        w_loaded = sem("w_loaded")
        zeroed_x = sem("zeroed_x")
        zeroed_dve = sem("zeroed_dve")
        zeroed_pool = sem("zeroed_pool")
        consts_ready = sem("consts_ready")
        wq_heads_ready = sem("wq_heads_ready")
        wv_heads_ready = sem("wv_heads_ready")
        woT_ready = sem("woT_ready")
        woT_copied = sem("woT_copied")
        products_ready = sem("products_ready")
        products_copied = sem("products_copied")

        ZEROED = 3 + G

        def groups(c, r, g):
            return c * CG + (G * r + g + 1)

        def pairs(c, r):
            return c * R + (r + 1)

        block = ctx.enter_context(nc.Block())

        @block.sync
        def _(sp):
            def load(c, k, first):
                if not first:
                    sp.wait_ge(ctx_ready, c * R + (k // G - R + 1))
                src = hist[c * CG + k]
                sp.dma_start(x[k][0:P:2, :, :], src[:, :, 0:T * D]).then_inc(x_loaded[k], 16)
                sp.dma_start(x[k][1:P:2, :, D:T * D], src[:, :, T * D:ROWS * D]).then_inc(x_loaded[k], 16)

            for dst, src in ((wq, w_q), (wk, w_k), (wv, w_v), (wo, w_o)):
                sp.dma_start(dst[:], src).then_inc(w_loaded, 16)
            for k in range(CG):
                sp.wait_ge(zeroed_x, k + 1)
                if k == G * 2:
                    sp.wait_ge(u_ready, 1)
                load(0, k, True)
            with sp.Fori(1, CHUNKS) as c:
                for k in range(CG):
                    load(c, k, False)

        @block.gpsimd
        def _(pool):
            def load_target(c):
                pool.dma_start(tgt[:], target.rearrange("(c p) d -> c p d", p=P)[c]).then_inc(tgt_loaded, 16)

            def load_mask(c):
                pool.dma_start(mask_in[:], mask.rearrange("(c p) l -> c p l", p=P)[c]).then_inc(mask_loaded, 16)

            def store_y(c):
                pool.wait_ge(y_copied, c + 1)
                pool.dma_start(y.rearrange("(c p) d -> c p d", p=P)[c], y_out[:]).then_inc(y_stored, 16)
                pool.wait_ge(y_stored, 16 * c + 16)
                pool.sem_inc(y_free, 1)

            load_target(0)
            load_mask(0)
            pool.sem_inc(y_free, 1)
            nc.gpsimd.memset(ident[:], 0.0).then_inc(zeroed_pool, 1)
            nc.gpsimd.memset(picks[:], 0.0).then_inc(zeroed_pool, 1)
            for r in range(R):
                nc.gpsimd.memset(keys[r][:], 0.0).then_inc(zeroed_pool, 1)
            nc.gpsimd.memset(maskbias[:, 0, :, 1], NEG).then_inc(zeroed_pool, 1)
            pool.wait_ge(zeroed_pool, R + 3)
            nc.gpsimd.affine_select(out=ident[:], in_=ident[:], compare_op=ALU.not_equal, fill=1.0, base=0,
                                    pattern=[[-1, P]], channel_multiplier=1).then_inc(consts_ready, 1)
            for b2 in range(2):
                view = picks[:, :, :, b2, b2, :, :].rearrange("p g s a h -> p (g s) a h")
                nc.gpsimd.affine_select(out=view, in_=view, compare_op=ALU.not_equal, fill=1.0, base=-b2,
                                        pattern=[[-8, CG * SUB], [-2, A], [0, H]],
                                        channel_multiplier=1).then_inc(consts_ready, 1)

            def chunk(c, first, last):
                if not last:
                    pool.wait_ge(u_ready, c + 1)
                    load_target(c + 1)
                    pool.wait_ge(maskbias_ready, c + 1)
                    load_mask(c + 1)
                if not first:
                    store_y(c - 1)

            chunk(0, True, False)
            with pool.Fori(1, CHUNKS - 1) as c:
                chunk(c, False, False)
            chunk(CHUNKS - 1, False, True)
            store_y(CHUNKS - 1)
            pool.wait_ge(y_stored, 16 * CHUNKS)

        @block.vector
        def _(dve):
            def transpose_rows(c, r, g, sub, first):
                k = G * r + g
                if sub == 0:
                    dve.wait_ge(x_loaded[k], c * 32 + 32)
                    if not (first and r < 2):
                        dve.wait_ge(scores_ready, groups(c, r - 2, g))
                op = nc.vector.transpose(xT[r % 2][g][:, sub].rearrange("p t b j -> p (t b j)"), x[k][:, sub])
                if sub == SUB - 1:
                    op.then_inc(xT_ready, 1)

            def row_bias(c, r, g):
                dve.wait_ge(scores_ready, groups(c, r, g))
                nc.vector.reduce_max(bias[:, g:g + 1], ps_scores[g][:, 0:SM], AX.X, negate=True).then_inc(bias_ready, 1)

            def invert(c, r, g):
                dve.wait_ge(exp_ready, groups(c, r, g))
                nc.vector.reciprocal(inverse[:, g:g + 1], total[:, g:g + 1]).then_inc(inverse_ready, 1)

            def transpose_probs(c, r, g, first):
                dve.wait_ge(probs_ready, groups(c, r, g))
                if not (first and r < 1):
                    dve.wait_ge(spread_ready, pairs(c, r - 1))
                nc.vector.transpose(probsT[:, g].rearrange("p t b a h -> p (t b a h)"),
                                    probs[g][:]).then_inc(probsT_ready, 1)

            def make_maskbias(c):
                dve.wait_ge(mask_loaded, 16 * c + 16)
                for half in range(2):
                    src = mask_in[:].rearrange("p (s r) -> p r s", s=SEG)[:, half * T:T + half * (T - 1), :]
                    last = nc.vector.tensor_scalar(maskbias[:, half:T, :, half], src, 0.0, NEG, ALU.is_equal,
                                                   ALU.mult)
                last.then_inc(maskbias_ready, 1)

            nc.vector.memset(x[0][:, :, 0:D], 0.0).then_inc(zeroed_x, 1)
            nc.vector.memset(wq_heads[:], 0.0).then_inc(zeroed_dve, 1)
            nc.vector.memset(wv_heads[:], 0.0).then_inc(zeroed_dve, 1)
            for k in range(1, CG):
                nc.vector.memset(x[k][:, :, 0:D], 0.0).then_inc(zeroed_x, 1)
            dve.wait_ge(w_loaded, 64)
            dve.wait_ge(zeroed_dve, 1)
            for h in range(H):
                rows = slice(HD * h, HD * h + HD)
                last = nc.vector.tensor_copy(wq_heads[rows, h, :], wq[rows, :])
            last.then_inc(wq_heads_ready, 1)
            for g in range(G):
                nc.vector.memset(probs[g][:, SE:SP], 0.0).then_inc(zeroed_dve, 1)
            nc.vector.memset(weights[:], 0.0).then_inc(zeroed_dve, 1)
            dve.wait_ge(consts_ready, 1)
            for sub in range(SUB):
                nc.vector.tensor_copy(spreads[:, sub], ident[:, 64 * sub:64 * sub + 64].rearrange(
                    "p (b t j) -> p t b j", b=2, t=2)).then_inc(zeroed_dve, 1)
            cols = ident[:].rearrange("p (s c) -> p s c", s=SUB)
            for b2 in range(2):
                nc.vector.reduce_sum(used_rows[:, b2:b2 + 1], cols[:, :, 48 * b2:48 * b2 + 16],
                                     AX.XY).then_inc(zeroed_dve, 1)
            dve.wait_ge(zeroed_dve, ZEROED + 4)
            nc.vector.tensor_tensor(used_rows[:, 2:3], used_rows[:, 0:1], used_rows[:, 1:2],
                                    ALU.add).then_inc(zeroed_dve, 1)
            dve.wait_ge(zeroed_dve, ZEROED + 5)
            for g in range(G):
                nc.vector.tensor_scalar(ps_scores[g][:, S:SE], used_rows[:, 2:3], NEG - PEAK, PEAK, ALU.mult, ALU.add)
                last = nc.vector.memset(ps_scores[g][:, SE:SM], FLOOR)
            last.then_inc(zeroed_dve, 1)
            dve.wait_ge(zeroed_pool, R + 3)
            make_maskbias(0)
            for g in range(G):
                for sub in range(SUB):
                    transpose_rows(0, 0, g, sub, True)
                if g == 0:
                    dve.wait_ge(u_ready, 1)
                    nc.vector.transpose(uT[:].rearrange("p n g s b -> p (n g s b)"), ps_u[:]).then_inc(uT_ready, 1)

            def chunk(c, first, last):
                for r in range(R):
                    ahead = not (last and r == R - 1)
                    c1, r1 = (c, r + 1) if r + 1 < R else (c + 1, 0)

                    def rows(g, sub):
                        if ahead:
                            transpose_rows(c1, r1, g, sub, first and r + 1 < R)

                    row_bias(c, r, 0)
                    rows(0, 0)
                    invert(c, r, 0)
                    if r == 2 and not last:
                        dve.wait_ge(u_ready, c + 2)
                        dve.wait_ge(keys_ready, pairs(c, R - 1))
                        nc.vector.transpose(uT[:].rearrange("p n g s b -> p (n g s b)"),
                                            ps_u[:]).then_inc(uT_ready, 1)
                    rows(0, 1)
                    transpose_probs(c, r, 0, first)
                    row_bias(c, r, 1)
                    rows(1, 0)
                    invert(c, r, 1)
                    if r == R - 1 and not last:
                        make_maskbias(c + 1)
                    rows(1, 1)
                    transpose_probs(c, r, 1, first)

            chunk(0, True, False)
            with dve.Fori(1, CHUNKS - 1) as c:
                chunk(c, False, False)
            chunk(CHUNKS - 1, False, True)

        @block.scalar
        def _(act):
            def copy_ctx(c, r, first):
                act.wait_ge(ctx_ready, pairs(c, r))
                if not (first and r < 1):
                    act.wait_ge(ctxT_ready, pairs(c, r - 1))
                nc.scalar.copy(ctx_rows[:], ps_ctx[:, 0:D]).then_inc(ctx_copied, 1)

            def copy_ctxT(c, r, first):
                act.wait_ge(ctxT_ready, pairs(c, r))
                if r % R == 0 and not (first and r == 0):
                    act.wait_ge(y_ready, c + r // R)
                n = (r % R) * G * GB
                nc.scalar.copy(ctxT[:, :, n:n + G * GB],
                               ps_ctxT[:, 0:P].rearrange("p (n h) -> p h n", h=H)).then_inc(ctxT_copied, 1)

            def place_weights(c, r):
                act.wait_ge(spread_ready, pairs(c, r))
                for odd in range(2):
                    for a in range(A):
                        rows = slice(HD * a, HD * a + HD)
                        dst = weights[rows, odd, :, :, :, 2 * H * a:2 * H * a + 2 * H].rearrange(
                            "p s g t m -> p (s g t) m")
                        src = ps_spread[rows, SUB * SPREAD * odd:SUB * SPREAD * (odd + 1)].rearrange(
                            "p (n m) -> p n m", m=2 * H)
                        last = nc.scalar.copy(dst, src)
                    last.then_inc(weights_ready, 1)

            def exponential(c, r, g, first):
                act.wait_ge(bias_ready, groups(c, r, g))
                if not (first and r < 1):
                    act.wait_ge(probsT_ready, groups(c, r - 1, g))
                nc.scalar.activation(probs[g][:, 0:SE], ps_scores[g][:, 0:SE], ACT.Exp, bias=bias[:, g:g + 1],
                                     accum_out=total[:, g:g + 1]).then_inc(exp_ready, 1)

            def normalize(c, r, g):
                act.wait_ge(inverse_ready, groups(c, r, g))
                nc.scalar.activation(probs[g][:, 0:SE], probs[g][:, 0:SE], ACT.Copy,
                                     scale=inverse[:, g:g + 1]).then_inc(probs_ready, 1)

            def copy_targetT(c, first):
                act.wait_ge(tgtT_ready, c + 1)
                if not first:
                    act.wait_ge(u_ready, c)
                nc.scalar.copy(tgtT[:].rearrange("p a g s b -> p a (g s) b"),
                               ps_misc[:, 0:P].rearrange("p (n a b) -> p a n b", a=A, b=2)).then_inc(tgtT_copied, 1)

            def copy_y(c):
                act.wait_ge(y_ready, c + 1)
                act.wait_ge(y_free, c + 1)
                nc.scalar.copy(y_out[:], ps_misc[:, 0:D]).then_inc(y_copied, 1)

            def make_keys(c, r):
                act.wait_ge(uT_ready, c + 1)
                for a in range(A):
                    rows = slice(HD * a, HD * a + HD)
                    for b2 in range(2):
                        dst = keys[r][rows, :, b2, :, 16 * b2 + H * a:16 * b2 + H * a + H]
                        src = uT[rows, :, G * r:G * r + G, :, b2].rearrange("p (h b) g s -> p (g s) b h", h=H)
                        last = nc.scalar.copy(dst, src)
                last.then_inc(keys_ready, 1)

            copy_targetT(0, True)
            act.wait_ge(w_loaded, 64)
            act.wait_ge(zeroed_dve, ZEROED)
            for h in range(H):
                rows = slice(HD * h, HD * h + HD)
                last = nc.scalar.copy(wv_heads[rows, h, :], wv[rows, :])
            last.then_inc(wv_heads_ready, 1)
            act.wait_ge(products_ready, 1)
            nc.scalar.mul(scoreW[:], ps_u[:], 1.0 / SCALE).then_inc(products_copied, 1)
            act.wait_ge(woT_ready, 1)
            nc.scalar.copy(woT[:], ps_ctxT[:, 0:P]).then_inc(woT_copied, 1)
            act.wait_ge(zeroed_pool, R + 3)
            make_keys(0, 0)
            act.wait_ge(products_ready, 2)
            nc.scalar.copy(outW[:], ps_product[:]).then_inc(products_copied, 1)
            make_keys(0, 1)
            make_keys(0, 2)

            def chunk(c, first, last):
                for r in range(R):
                    if not (first and r < 2):
                        copy_ctx(c, r - 2, first)
                    exponential(c, r, 0, first)
                    if not (first and r < 1):
                        place_weights(c, r - 1)
                    normalize(c, r, 0)
                    if r == 1 and not last:
                        copy_targetT(c + 1, False)
                    if r == 2 and not first:
                        copy_y(c - 1)
                    if not (first and r < 2):
                        copy_ctxT(c, r - 2, first)
                    exponential(c, r, 1, first)
                    normalize(c, r, 1)
                    if r == 0:
                        make_keys(c, R - 1)
                    elif r == 2 and not last:
                        make_keys(c + 1, 0)
                        make_keys(c + 1, 1)
                    elif r == 3 and not last:
                        make_keys(c + 1, 2)

            chunk(0, True, False)
            with act.Fori(1, CHUNKS - 1) as c:
                chunk(c, False, False)
            chunk(CHUNKS - 1, False, True)
            copy_ctx(CHUNKS - 1, R - 2, False)
            place_weights(CHUNKS - 1, R - 1)
            copy_ctxT(CHUNKS - 1, R - 2, False)
            copy_ctx(CHUNKS - 1, R - 1, False)
            copy_ctxT(CHUNKS - 1, R - 1, False)
            copy_y(CHUNKS - 1)

        @block.tensor
        def _(pe):
            def scores(c, r, g, first):
                pe.wait_ge(xT_ready, groups(c, r, g))
                if g == 0:
                    pe.wait_ge(keys_ready, pairs(c, r))
                if g == 0 and r == 0:
                    pe.wait_ge(maskbias_ready, c + 1)
                if not (first and r < 1):
                    pe.wait_ge(exp_ready, groups(c, r - 1, g))
                for q in range(Q):
                    sub, b2 = q // 2, q % 2
                    nc.tensor.matmul(ps_scores[g][HD * q:HD * q + HD, 0:S],
                                     picks[:, G * r + g, sub, b2, :, :, :].rearrange("p b a h -> p (b a h)"),
                                     maskbias[:].rearrange("p t s f -> p (t s f)"),
                                     start=True, stop=False, tile_position=(0, HD * q))
                for b in range(NB):
                    for q in range(Q):
                        sub, b2 = q // 2, q % 2
                        last = nc.tensor.matmul(ps_scores[g][HD * q:HD * q + HD, 0:S],
                                                keys[r][:, SUB * g + sub, b2, b, :],
                                                xT[r % 2][g][:, sub, :, b, JJ * b2:JJ * b2 + JJ],
                                                start=False, stop=(b == NB - 1), tile_position=(0, HD * q))
                last.then_inc(scores_ready, 1)

            def spread(c, r, first):
                for g in range(G):
                    pe.wait_ge(probsT_ready, groups(c, r, g))
                if not (first and r < 1):
                    pe.wait_ge(weights_ready, 2 * pairs(c, r - 1))
                for odd in range(2):
                    for sub in range(SUB):
                        n = SPREAD * (SUB * odd + sub)
                        for a in range(A):
                            last = nc.tensor.matmul(ps_spread[HD * a:HD * a + HD, n:n + SPREAD],
                                                    spreads[:, sub, odd, :, :].rearrange("p b j -> p (b j)"),
                                                    probsT[:, :, :, :, a, :].rearrange("p g t b h -> p (g t) b h"),
                                                    start=True, stop=True, tile_position=(0, HD * a))
                last.then_inc(spread_ready, 1)

            def weighted(c, r, first):
                if not (first and r < 1):
                    pe.wait_ge(ctx_copied, pairs(c, r - 1))
                steps = [*range(0, T, 2), *range(1, T, 2)]
                for t in steps:
                    if t < 2:
                        pe.wait_ge(weights_ready, 2 * pairs(c, r) - 1 + t)
                    for g in range(G):
                        for sub in range(SUB):
                            q = SUB * g + sub
                            last = nc.tensor.matmul(ps_ctx[HD * q:HD * q + HD, 0:D],
                                                    weights[:, t % 2, sub, g, t // 2, :],
                                                    x[G * (r % R) + g][:, sub, t * D:t * D + D],
                                                    start=(t == steps[0]), stop=(t == steps[-1]),
                                                    tile_position=(0, HD * q))
                last.then_inc(ctx_ready, 1)

            def transpose_ctx(c, r, first):
                pe.wait_ge(ctx_copied, pairs(c, r))
                if not (first and r < 1):
                    pe.wait_ge(ctxT_copied, pairs(c, r - 1))
                nc.tensor.transpose(ps_ctxT[:, 0:P], ctx_rows[:], ident[:]).then_inc(ctxT_ready, 1)

            def transpose_target(c):
                pe.wait_ge(tgt_loaded, 16 * c + 16)
                nc.tensor.transpose(ps_misc[:, 0:P], tgt[:], ident[:]).then_inc(tgtT_ready, 1)

            def score_vectors(c):
                pe.wait_ge(tgtT_copied, c + 1)
                nc.tensor.matmul(ps_u[:], tgtT[:].rearrange("p a g s b -> p (a g s b)"), scoreW[:],
                                 start=True, stop=True).then_inc(u_ready, 1)

            def project(c):
                pe.wait_ge(ctxT_copied, pairs(c, R - 1))
                for h in range(H):
                    last = nc.tensor.matmul(ps_misc[:, 0:D], ctxT[:, h, :], outW[:, h * D:h * D + D],
                                            start=(h == 0), stop=(h == H - 1))
                last.then_inc(y_ready, 1)

            pe.wait_ge(consts_ready, 3)
            transpose_target(0)
            pe.wait_ge(wq_heads_ready, 1)
            for h in range(H):
                last = nc.tensor.matmul(ps_u[:, h * D:h * D + D], wq_heads[:, h, :], wk[:], start=True, stop=True)
            last.then_inc(products_ready, 1)
            nc.tensor.transpose(ps_ctxT[:, 0:P], wo[:], ident[:]).then_inc(woT_ready, 1)
            pe.wait_ge(products_copied, 1)
            score_vectors(0)
            pe.wait_ge(woT_copied, 1)
            pe.wait_ge(wv_heads_ready, 1)
            for h in range(H):
                last = nc.tensor.matmul(ps_product[:, h * D:h * D + D], wv_heads[:, h, :], woT[:], start=True, stop=True)
            last.then_inc(products_ready, 1)
            pe.wait_ge(zeroed_dve, ZEROED + 6)

            def chunk(c, first, last):
                for r in range(R):
                    scores(c, r, 0, first)
                    if r == 1 and not last:
                        transpose_target(c + 1)
                    if r == 2 and not first:
                        pe.wait_ge(tgtT_copied, c + 1 if last else c + 2)
                        project(c - 1)
                    if not (first and r < 2):
                        transpose_ctx(c, r - 2, first)
                    if not (first and r < 1):
                        spread(c, r - 1, first)
                    scores(c, r, 1, first)
                    if not (first and r < 1):
                        weighted(c, r - 1, first)
                    if r == 1 and not last:
                        pe.wait_ge(uT_ready, c + 1)
                        score_vectors(c + 1)

            chunk(0, True, False)
            with pe.Fori(1, CHUNKS - 1) as c:
                chunk(c, False, False)
            chunk(CHUNKS - 1, False, True)
            spread(CHUNKS - 1, R - 1, False)
            transpose_ctx(CHUNKS - 1, R - 2, False)
            weighted(CHUNKS - 1, R - 1, False)
            transpose_ctx(CHUNKS - 1, R - 1, False)
            pe.wait_ge(y_copied, CHUNKS - 1)
            project(CHUNKS - 1)


_INS = ["r_target_item", "r_history_sequence", "r_mask", "L0_rec_W_q", "L0_rec_W_k", "L0_rec_W_v", "L0_rec_W_o"]


def kernel(**inputs):
    import concourse.bacc as bacc
    import numpy as np
    from concourse.bass_utils import run_bass_kernel_spmd

    nc = bacc.Bacc("TRN2", target_bir_lowering=False, num_devices=1)
    arrays, args = {}, []
    for name in _INS:
        a = np.ascontiguousarray(inputs[name])
        arrays[name] = a
        args.append(nc.dram_tensor(name, a.shape, mybir.dt.from_np(a.dtype), kind="ExternalInput").ap())
    y = nc.dram_tensor("y", inputs["r_target_item"].shape, mybir.dt.float32, kind="ExternalOutput").ap()
    target_attention(nc, *args, y)
    return run_bass_kernel_spmd(nc, [arrays], core_ids=[0]).results[0]["y"]
```

```python
from contextlib import ExitStack

import concourse.bass as bass
from concourse import mybir


def target_attention(nc, target, history, mask, w_q, w_k, w_v, w_o, y):
    F32 = mybir.dt.float32
    BF16 = mybir.dt.bfloat16
    I32 = mybir.dt.int32
    ALU = mybir.AluOpType
    ACT = mybir.ActivationFunctionType
    AX = mybir.AxisListType

    B, D = target.shape
    L = mask.shape[1]
    P = 128
    HD = 32
    H = D // HD
    NB = D // HD
    A = P // HD
    SEG = 8
    ROWS = L // SEG
    T = (ROWS + 1) // 2
    JJ = 2 * SEG
    SUB = 2
    GB = SUB * P // JJ
    G = 2
    R = P // (G * GB)
    CG = R * G
    CHUNKS = B // P
    PAIRS = CHUNKS * R
    Q = 2 * SUB
    S = T * JJ
    TP = (T + 1) // 2
    SP = TP * HD
    SPREAD = G * TP * 2 * H
    NEG = -3.0e38
    FLOOR = -1.0e37
    PEAK = 1.0e30
    SE = S + 1
    SM = S + 2
    SCALE = HD ** 0.5
    assert CG * GB == P and PAIRS * G * GB == B and GB == 2 * P // JJ

    hist = history.rearrange("b l d -> (b l) d").rearrange("(n u s r) d -> n s u (r d)", u=SUB, s=P // 2, r=ROWS)

    ctx = ExitStack()
    with ctx:
        def sb(name, shape, dt=F32):
            return ctx.enter_context(nc.sbuf_tensor(name, shape, dt))

        def bank(name, width=512):
            return ctx.enter_context(nc.psum_tensor(name, [P, width], F32))

        def sem(name):
            return ctx.enter_context(nc.semaphore(name))

        x = [sb(f"x{k}", [P, SUB, T * D]) for k in range(CG)]
        xT = [[sb(f"xT{k}{g}", [P, SUB, T, NB, HD]) for g in range(G)] for k in range(2)]
        keys = [sb(f"keys{r}", [P, G * SUB, 2, NB, HD]) for r in range(R)]
        uT = sb("uT", [P, NB * H, CG, SUB, 2])
        probs = [sb(f"probs{g}", [P, SP]) for g in range(G)]
        probsT = sb("probsT", [P, G, TP, 2, A, H])
        weights = sb("weights", [P, 2, SUB, G, TP, HD])
        bias = sb("bias", [P, G])
        total = sb("total", [P, G])
        inverse = sb("inverse", [P, G])
        used_rows = sb("used_rows", [P, 3])
        mask_in = sb("mask_in", [P, L], I32)
        maskbias = sb("maskbias", [P, T, SEG, 2], BF16)
        picks = sb("picks", [P, CG, SUB, 2, 2, A, H], BF16)
        ident = sb("ident", [P, P])
        spreads = sb("spreads", [P, SUB, 2, 2, JJ])
        tgt = sb("tgt", [P, D])
        tgtT = sb("tgtT", [P, A, CG, SUB, 2])
        ctx_rows = sb("ctx_rows", [P, D])
        ctxT = sb("ctxT", [P, H, P])
        y_out = sb("y_out", [P, D])
        scoreW = sb("scoreW", [P, H * D])
        outW = sb("outW", [P, H * D])
        wq = sb("wq", [P, D])
        wk = sb("wk", [P, D])
        wv = sb("wv", [P, D])
        wo = sb("wo", [P, D])
        woT = sb("woT", [P, D])
        wq_heads = sb("wq_heads", [P, H, D])
        wv_heads = sb("wv_heads", [P, H, D])

        ps_scores = [bank(f"ps_scores{g}") for g in range(G)]
        ps_spread = bank("ps_spread")
        ps_product = bank("ps_product")
        ps_ctx = bank("ps_ctx")
        ps_ctxT = bank("ps_ctxT")
        ps_u = bank("ps_u")
        ps_misc = bank("ps_misc")

        x_loaded = [sem(f"x_loaded{k}") for k in range(CG)]
        xT_ready = sem("xT_ready")
        scores_ready = sem("scores_ready")
        bias_ready = sem("bias_ready")
        exp_ready = sem("exp_ready")
        inverse_ready = sem("inverse_ready")
        probs_ready = sem("probs_ready")
        probsT_ready = sem("probsT_ready")
        spread_ready = sem("spread_ready")
        weights_ready = sem("weights_ready")
        ctx_ready = sem("ctx_ready")
        ctx_copied = sem("ctx_copied")
        ctxT_ready = sem("ctxT_ready")
        ctxT_copied = sem("ctxT_copied")
        keys_ready = sem("keys_ready")
        tgt0_loaded = sem("tgt0_loaded")
        tgt_loaded = sem("tgt_loaded")
        tgtT_ready = sem("tgtT_ready")
        tgtT_copied = sem("tgtT_copied")
        u_ready = sem("u_ready")
        uT_ready = sem("uT_ready")
        mask0_loaded = sem("mask0_loaded")
        mask_loaded = sem("mask_loaded")
        maskbias_ready = sem("maskbias_ready")
        y_ready = sem("y_ready")
        y_copied = sem("y_copied")
        y_stored = sem("y_stored")
        y_free = sem("y_free")
        wqk_loaded = sem("wqk_loaded")
        wvo_loaded = sem("wvo_loaded")
        zeroed_x = sem("zeroed_x")
        zeroed_dve = sem("zeroed_dve")
        zeroed_pool = sem("zeroed_pool")
        consts_ready = sem("consts_ready")
        wq_heads_ready = sem("wq_heads_ready")
        wv_heads_ready = sem("wv_heads_ready")
        woT_ready = sem("woT_ready")
        woT_copied = sem("woT_copied")
        products_ready = sem("products_ready")
        products_copied = sem("products_copied")

        ZEROED = 2 + G

        def groups(c, r, g):
            return c * CG + (G * r + g + 1)

        def pairs(c, r):
            return c * R + (r + 1)

        block = ctx.enter_context(nc.Block())

        @block.sync
        def _(sp):
            def load(c, k, first):
                if not first:
                    sp.wait_ge(ctx_ready, c * R + (k // G - R + 1))
                src = hist[c * CG + k]
                sp.dma_start(x[k][0:P:2, :, :], src[:, :, 0:T * D]).then_inc(x_loaded[k], 16)
                sp.dma_start(x[k][1:P:2, :, D:T * D], src[:, :, T * D:ROWS * D]).then_inc(x_loaded[k], 16)

            def load_target(c):
                sp.wait_ge(u_ready, c)
                sp.dma_start(tgt[:], target.rearrange("(c p) d -> c p d", p=P)[c]).then_inc(tgt_loaded, 16)

            def load_mask(c):
                sp.wait_ge(maskbias_ready, c)
                sp.dma_start(mask_in[:], mask.rearrange("(c p) l -> c p l", p=P)[c]).then_inc(mask_loaded, 16)

            def chunk(c, last):
                for k in range(CG):
                    load(c, k, False)
                    if k == 0 and not last:
                        load_target(c + 1)
                if not last:
                    load_mask(c + 1)

            for dst, src in ((wq, w_q), (wk, w_k)):
                sp.dma_start(dst[:], src).then_inc(wqk_loaded, 16)
            for k in range(CG):
                sp.wait_ge(zeroed_x, k + 1)
                load(0, k, True)
                if k == 0:
                    for dst, src in ((wv, w_v), (wo, w_o)):
                        sp.dma_start(dst[:], src).then_inc(wvo_loaded, 16)
                if k == CG // 2 - 1:
                    load_target(1)
                    load_mask(1)
            with sp.Fori(1, CHUNKS - 1) as c:
                chunk(c, False)
            chunk(CHUNKS - 1, True)

        @block.gpsimd
        def _(pool):
            def store_y(c):
                pool.wait_ge(y_copied, c + 1)
                pool.dma_start(y.rearrange("(c p) d -> c p d", p=P)[c], y_out[:]).then_inc(y_stored, 16)
                pool.wait_ge(y_stored, 16 * c + 16)
                pool.sem_inc(y_free, 1)

            pool.dma_start(tgt[:], target.rearrange("(c p) d -> c p d", p=P)[0]).then_inc(tgt0_loaded, 16)
            pool.dma_start(mask_in[:], mask.rearrange("(c p) l -> c p l", p=P)[0]).then_inc(mask0_loaded, 16)
            pool.sem_inc(y_free, 1)
            nc.gpsimd.memset(ident[:], 0.0).then_inc(zeroed_pool, 1)
            pool.wait_ge(zeroed_pool, 1)
            nc.gpsimd.affine_select(out=ident[:], in_=ident[:], compare_op=ALU.not_equal, fill=1.0, base=0,
                                    pattern=[[-1, P]], channel_multiplier=1).then_inc(consts_ready, 1)
            nc.gpsimd.memset(maskbias[:, 0, :, 1], NEG).then_inc(zeroed_pool, 1)
            nc.gpsimd.memset(picks[:], 0.0).then_inc(zeroed_pool, 1)
            nc.gpsimd.memset(keys[0][:], 0.0).then_inc(zeroed_pool, 1)
            pool.wait_ge(zeroed_pool, 3)
            for b2 in range(2):
                view = picks[:, :, :, b2, b2, :, :].rearrange("p g s a h -> p (g s) a h")
                nc.gpsimd.affine_select(out=view, in_=view, compare_op=ALU.not_equal, fill=1.0, base=-b2,
                                        pattern=[[-8, CG * SUB], [-2, A], [0, H]],
                                        channel_multiplier=1).then_inc(consts_ready, 1)
            for r in range(1, R):
                nc.gpsimd.memset(keys[r][:], 0.0).then_inc(zeroed_pool, 1)

            with pool.Fori(0, CHUNKS) as c:
                store_y(c)
            pool.wait_ge(y_stored, 16 * CHUNKS)

        @block.vector
        def _(dve):
            def transpose_rows(c, r, g, sub, first):
                k = G * r + g
                if sub == 0:
                    dve.wait_ge(x_loaded[k], c * 32 + 32)
                    if not (first and r < 2):
                        dve.wait_ge(scores_ready, groups(c, r - 2, g))
                op = nc.vector.transpose(xT[r % 2][g][:, sub].rearrange("p t b j -> p (t b j)"), x[k][:, sub])
                if sub == SUB - 1:
                    op.then_inc(xT_ready, 1)

            def row_bias(c, r, g):
                dve.wait_ge(scores_ready, groups(c, r, g))
                nc.vector.reduce_max(bias[:, g:g + 1], ps_scores[g][:, 0:SM], AX.X, negate=True).then_inc(bias_ready, 1)

            def invert(c, r, g):
                dve.wait_ge(exp_ready, groups(c, r, g))
                nc.vector.reciprocal(inverse[:, g:g + 1], total[:, g:g + 1]).then_inc(inverse_ready, 1)

            def transpose_probs(c, r, g, first):
                dve.wait_ge(probs_ready, groups(c, r, g))
                if not (first and r < 1):
                    dve.wait_ge(spread_ready, pairs(c, r - 1))
                nc.vector.transpose(probsT[:, g].rearrange("p t b a h -> p (t b a h)"),
                                    probs[g][:]).then_inc(probsT_ready, 1)

            def make_maskbias(c, first):
                if first:
                    dve.wait_ge(mask0_loaded, 16)
                else:
                    dve.wait_ge(mask_loaded, 16 * c)
                for half in range(2):
                    src = mask_in[:].rearrange("p (s r) -> p r s", s=SEG)[:, half * T:T + half * (T - 1), :]
                    last = nc.vector.tensor_scalar(maskbias[:, half:T, :, half], src, 0.0, NEG, ALU.is_equal,
                                                   ALU.mult)
                last.then_inc(maskbias_ready, 1)

            nc.vector.memset(x[0][:, :, 0:D], 0.0).then_inc(zeroed_x, 1)
            nc.vector.memset(wq_heads[:], 0.0).then_inc(zeroed_dve, 1)
            nc.vector.memset(x[1][:, :, 0:D], 0.0).then_inc(zeroed_x, 1)
            nc.vector.memset(wv_heads[:], 0.0).then_inc(zeroed_dve, 1)
            dve.wait_ge(wqk_loaded, 32)
            dve.wait_ge(zeroed_dve, 1)
            for h in range(H):
                rows = slice(HD * h, HD * h + HD)
                last = nc.vector.tensor_copy(wq_heads[rows, h, :], wq[rows, :])
            last.then_inc(wq_heads_ready, 1)
            for k in range(2, CG):
                nc.vector.memset(x[k][:, :, 0:D], 0.0).then_inc(zeroed_x, 1)
            for g in range(G):
                nc.vector.memset(probs[g][:, SE:SP], 0.0).then_inc(zeroed_dve, 1)
            dve.wait_ge(consts_ready, 1)
            cols = ident[:].rearrange("p (s c) -> p s c", s=SUB)
            for b2 in range(2):
                nc.vector.reduce_sum(used_rows[:, b2:b2 + 1], cols[:, :, 48 * b2:48 * b2 + 16],
                                     AX.XY).then_inc(zeroed_dve, 1)
            for sub in range(SUB):
                nc.vector.tensor_copy(spreads[:, sub], ident[:, 64 * sub:64 * sub + 64].rearrange(
                    "p (b t j) -> p t b j", b=2, t=2)).then_inc(zeroed_dve, 1)
            dve.wait_ge(zeroed_dve, ZEROED + 2)
            nc.vector.tensor_tensor(used_rows[:, 2:3], used_rows[:, 0:1], used_rows[:, 1:2],
                                    ALU.add).then_inc(zeroed_dve, 1)
            dve.wait_ge(zeroed_pool, 2)
            make_maskbias(0, True)
            dve.wait_ge(zeroed_dve, ZEROED + 5)
            for g in range(G):
                nc.vector.tensor_scalar(ps_scores[g][:, S:SE], used_rows[:, 2:3], NEG - PEAK, PEAK, ALU.mult, ALU.add)
                last = nc.vector.memset(ps_scores[g][:, SE:SM], FLOOR)
            last.then_inc(zeroed_dve, 1)
            nc.vector.memset(weights[:], 0.0).then_inc(zeroed_dve, 1)
            for g in range(G):
                for sub in range(SUB):
                    transpose_rows(0, 0, g, sub, True)
                    if g == 0 and sub == 0:
                        dve.wait_ge(u_ready, 1)
                        nc.vector.transpose(uT[:].rearrange("p n g s b -> p (n g s b)"), ps_u[:]).then_inc(uT_ready, 1)

            def chunk(c, first, last):
                for r in range(R):
                    ahead = not (last and r == R - 1)
                    c1, r1 = (c, r + 1) if r + 1 < R else (c + 1, 0)

                    def rows(g, sub):
                        if ahead:
                            transpose_rows(c1, r1, g, sub, first and r + 1 < R)

                    row_bias(c, r, 0)
                    rows(0, 0)
                    invert(c, r, 0)
                    if r == 2 and not last:
                        dve.wait_ge(u_ready, c + 2)
                        dve.wait_ge(keys_ready, pairs(c, R - 1))
                        nc.vector.transpose(uT[:].rearrange("p n g s b -> p (n g s b)"),
                                            ps_u[:]).then_inc(uT_ready, 1)
                    rows(0, 1)
                    transpose_probs(c, r, 0, first)
                    row_bias(c, r, 1)
                    if r == R - 1 and not last:
                        make_maskbias(c + 1, False)
                    rows(1, 0)
                    invert(c, r, 1)
                    rows(1, 1)
                    transpose_probs(c, r, 1, first)

            chunk(0, True, False)
            with dve.Fori(1, CHUNKS - 1) as c:
                chunk(c, False, False)
            chunk(CHUNKS - 1, False, True)

        @block.scalar
        def _(act):
            def copy_ctx(c, r, first):
                act.wait_ge(ctx_ready, pairs(c, r))
                if not (first and r < 1):
                    act.wait_ge(ctxT_ready, pairs(c, r - 1))
                nc.scalar.copy(ctx_rows[:], ps_ctx[:, 0:D]).then_inc(ctx_copied, 1)

            def copy_ctxT(c, r, first):
                act.wait_ge(ctxT_ready, pairs(c, r))
                if r % R == 0 and not (first and r == 0):
                    act.wait_ge(y_ready, c + r // R)
                n = (r % R) * G * GB
                nc.scalar.copy(ctxT[:, :, n:n + G * GB],
                               ps_ctxT[:, 0:P].rearrange("p (n h) -> p h n", h=H)).then_inc(ctxT_copied, 1)

            def place_weights(c, r, odd):
                act.wait_ge(spread_ready, pairs(c, r))
                for a in range(A):
                    rows = slice(HD * a, HD * a + HD)
                    dst = weights[rows, odd, :, :, :, 2 * H * a:2 * H * a + 2 * H].rearrange("p s g t m -> p (s g t) m")
                    src = ps_spread[rows, SUB * SPREAD * odd:SUB * SPREAD * (odd + 1)].rearrange(
                        "p (n m) -> p n m", m=2 * H)
                    last = nc.scalar.copy(dst, src)
                last.then_inc(weights_ready, 1)

            def exponential(c, r, g, first):
                act.wait_ge(bias_ready, groups(c, r, g))
                if not (first and r < 1):
                    act.wait_ge(probsT_ready, groups(c, r - 1, g))
                nc.scalar.activation(probs[g][:, 0:SE], ps_scores[g][:, 0:SE], ACT.Exp, bias=bias[:, g:g + 1],
                                     accum_out=total[:, g:g + 1]).then_inc(exp_ready, 1)

            def normalize(c, r, g):
                act.wait_ge(inverse_ready, groups(c, r, g))
                nc.scalar.activation(probs[g][:, 0:SE], probs[g][:, 0:SE], ACT.Copy,
                                     scale=inverse[:, g:g + 1]).then_inc(probs_ready, 1)

            def copy_targetT(c, first):
                act.wait_ge(tgtT_ready, c + 1)
                if not first:
                    act.wait_ge(u_ready, c)
                nc.scalar.copy(tgtT[:].rearrange("p a g s b -> p a (g s) b"),
                               ps_misc[:, 0:P].rearrange("p (n a b) -> p a n b", a=A, b=2)).then_inc(tgtT_copied, 1)

            def copy_y(c):
                act.wait_ge(y_ready, c + 1)
                act.wait_ge(y_free, c + 1)
                nc.scalar.copy(y_out[:], ps_misc[:, 0:D]).then_inc(y_copied, 1)

            def make_keys(c, r):
                act.wait_ge(uT_ready, c + 1)
                for a in range(A):
                    rows = slice(HD * a, HD * a + HD)
                    for b2 in range(2):
                        dst = keys[r][rows, :, b2, :, 16 * b2 + H * a:16 * b2 + H * a + H]
                        src = uT[rows, :, G * r:G * r + G, :, b2].rearrange("p (h b) g s -> p (g s) b h", h=H)
                        last = nc.scalar.copy(dst, src)
                last.then_inc(keys_ready, 1)

            copy_targetT(0, True)
            act.wait_ge(products_ready, 1)
            nc.scalar.mul(scoreW[:], ps_u[:], 1.0 / SCALE).then_inc(products_copied, 1)
            act.wait_ge(wvo_loaded, 32)
            act.wait_ge(zeroed_dve, 2)
            for h in range(H):
                rows = slice(HD * h, HD * h + HD)
                last = nc.scalar.copy(wv_heads[rows, h, :], wv[rows, :])
            last.then_inc(wv_heads_ready, 1)
            act.wait_ge(woT_ready, 1)
            nc.scalar.copy(woT[:], ps_ctxT[:, 0:P]).then_inc(woT_copied, 1)
            act.wait_ge(zeroed_pool, 4)
            make_keys(0, 0)
            act.wait_ge(zeroed_pool, R + 3)
            make_keys(0, 1)

            def chunk(c, first, last):
                for r in range(R):
                    end = last and r == R - 1
                    exponential(c, r, 0, first)
                    if end:
                        normalize(c, r, 0)
                    if not (first and r < 2):
                        copy_ctx(c, r - 2, first)
                    if first and r == 1:
                        act.wait_ge(zeroed_dve, ZEROED + 7)
                    if not (first and r < 1):
                        place_weights(c, r - 1, 0)
                    if not end:
                        normalize(c, r, 0)
                    if not (first and r < 1):
                        place_weights(c, r - 1, 1)
                    if r == (1 if first else 0) and not last:
                        copy_targetT(c + 1, False)
                    exponential(c, r, 1, first)
                    normalize(c, r, 1)
                    if r == 2 and not first:
                        copy_y(c - 1)
                    if not (first and r < 2):
                        copy_ctxT(c, r - 2, first)
                    if first and r == 0:
                        act.wait_ge(products_ready, 2)
                        nc.scalar.copy(outW[:], ps_product[:]).then_inc(products_copied, 1)
                        make_keys(c, R - 2)
                    if r == 0:
                        make_keys(c, R - 1)
                    elif r == 2 and not last:
                        make_keys(c + 1, 0)
                        make_keys(c + 1, 1)
                    elif r == 3 and not last:
                        make_keys(c + 1, 2)

            chunk(0, True, False)
            with act.Fori(1, CHUNKS - 1) as c:
                chunk(c, False, False)
            chunk(CHUNKS - 1, False, True)
            place_weights(CHUNKS - 1, R - 1, 0)
            copy_ctx(CHUNKS - 1, R - 2, False)
            place_weights(CHUNKS - 1, R - 1, 1)
            copy_ctxT(CHUNKS - 1, R - 2, False)
            copy_ctx(CHUNKS - 1, R - 1, False)
            copy_ctxT(CHUNKS - 1, R - 1, False)
            copy_y(CHUNKS - 1)

        @block.tensor
        def _(pe):
            def scores(c, r, g, first):
                pe.wait_ge(xT_ready, groups(c, r, g))
                if g == 0:
                    pe.wait_ge(keys_ready, pairs(c, r))
                if g == 0 and r == 0:
                    pe.wait_ge(maskbias_ready, c + 1)
                if not (first and r < 1):
                    pe.wait_ge(exp_ready, groups(c, r - 1, g))
                for q in range(Q):
                    sub, b2 = q // 2, q % 2
                    nc.tensor.matmul(ps_scores[g][HD * q:HD * q + HD, 0:S],
                                     picks[:, G * r + g, sub, b2, :, :, :].rearrange("p b a h -> p (b a h)"),
                                     maskbias[:].rearrange("p t s f -> p (t s f)"),
                                     start=True, stop=False, tile_position=(0, HD * q))
                for b in range(NB):
                    for q in range(Q):
                        sub, b2 = q // 2, q % 2
                        last = nc.tensor.matmul(ps_scores[g][HD * q:HD * q + HD, 0:S],
                                                keys[r][:, SUB * g + sub, b2, b, :],
                                                xT[r % 2][g][:, sub, :, b, JJ * b2:JJ * b2 + JJ],
                                                start=False, stop=(b == NB - 1), tile_position=(0, HD * q))
                last.then_inc(scores_ready, 1)

            def spread(c, r, first):
                for g in range(G):
                    pe.wait_ge(probsT_ready, groups(c, r, g))
                if not (first and r < 1):
                    pe.wait_ge(weights_ready, 2 * pairs(c, r - 1))
                for odd in range(2):
                    for sub in range(SUB):
                        n = SPREAD * (SUB * odd + sub)
                        for a in range(A):
                            last = nc.tensor.matmul(ps_spread[HD * a:HD * a + HD, n:n + SPREAD],
                                                    spreads[:, sub, odd, :, :].rearrange("p b j -> p (b j)"),
                                                    probsT[:, :, :, :, a, :].rearrange("p g t b h -> p (g t) b h"),
                                                    start=True, stop=True, tile_position=(0, HD * a))
                last.then_inc(spread_ready, 1)

            def weighted(c, r, odd, first):
                if not odd and not (first and r < 1):
                    pe.wait_ge(ctx_copied, pairs(c, r - 1))
                pe.wait_ge(weights_ready, 2 * pairs(c, r) - 1 + odd)
                for t in range(odd, T, 2):
                    for g in range(G):
                        for sub in range(SUB):
                            q = SUB * g + sub
                            last = nc.tensor.matmul(ps_ctx[HD * q:HD * q + HD, 0:D],
                                                    weights[:, odd, sub, g, t // 2, :],
                                                    x[G * (r % R) + g][:, sub, t * D:t * D + D],
                                                    start=(t == 0), stop=(odd == 1 and t + 2 >= T),
                                                    tile_position=(0, HD * q))
                if odd:
                    last.then_inc(ctx_ready, 1)

            def transpose_ctx(c, r, first):
                pe.wait_ge(ctx_copied, pairs(c, r))
                if not (first and r < 1):
                    pe.wait_ge(ctxT_copied, pairs(c, r - 1))
                nc.tensor.transpose(ps_ctxT[:, 0:P], ctx_rows[:], ident[:]).then_inc(ctxT_ready, 1)

            def transpose_target(c, first):
                if first:
                    pe.wait_ge(tgt0_loaded, 16)
                else:
                    pe.wait_ge(tgt_loaded, 16 * c)
                nc.tensor.transpose(ps_misc[:, 0:P], tgt[:], ident[:]).then_inc(tgtT_ready, 1)

            def score_vectors(c):
                pe.wait_ge(tgtT_copied, c + 1)
                nc.tensor.matmul(ps_u[:], tgtT[:].rearrange("p a g s b -> p (a g s b)"), scoreW[:],
                                 start=True, stop=True).then_inc(u_ready, 1)

            def project(c):
                pe.wait_ge(ctxT_copied, pairs(c, R - 1))
                for h in range(H):
                    last = nc.tensor.matmul(ps_misc[:, 0:D], ctxT[:, h, :], outW[:, h * D:h * D + D],
                                            start=(h == 0), stop=(h == H - 1))
                last.then_inc(y_ready, 1)

            def output_matrix():
                pe.wait_ge(woT_copied, 1)
                pe.wait_ge(wv_heads_ready, 1)
                for h in range(H):
                    last = nc.tensor.matmul(ps_product[:, h * D:h * D + D], wv_heads[:, h, :], woT[:],
                                            start=True, stop=True)
                last.then_inc(products_ready, 1)

            pe.wait_ge(wq_heads_ready, 1)
            for h in range(H):
                last = nc.tensor.matmul(ps_u[:, h * D:h * D + D], wq_heads[:, h, :], wk[:], start=True, stop=True)
            last.then_inc(products_ready, 1)
            pe.wait_ge(consts_ready, 1)
            transpose_target(0, True)
            pe.wait_ge(products_copied, 1)
            score_vectors(0)
            pe.wait_ge(wvo_loaded, 32)
            nc.tensor.transpose(ps_ctxT[:, 0:P], wo[:], ident[:]).then_inc(woT_ready, 1)
            pe.wait_ge(consts_ready, 3)
            pe.wait_ge(zeroed_dve, ZEROED + 6)
            scores(0, 0, 0, True)

            def chunk(c, first, last):
                for r in range(R):
                    c1, r1 = (c, r + 1) if r + 1 < R else (c + 1, 0)
                    if not (first and r < 1):
                        spread(c, r - 1, first)
                    if r == (1 if first else 0) and not last:
                        transpose_target(c + 1, False)
                    if not (first and r < 2):
                        if first and r == 2:
                            pe.wait_ge(woT_copied, 1)
                        transpose_ctx(c, r - 2, first)
                    scores(c, r, 1, first)
                    if r == 2 and not first:
                        pe.wait_ge(tgtT_copied, c + 1 if last else c + 2)
                        project(c - 1)
                    if first and r == 0:
                        output_matrix()
                    if not (first and r < 1):
                        weighted(c, r - 1, 0, first)
                    if last and r == R - 1:
                        spread(c, r, False)
                    else:
                        scores(c1, r1, 0, False)
                    if not (first and r < 1):
                        weighted(c, r - 1, 1, first)
                    if r == (1 if first else 0) and not last:
                        pe.wait_ge(uT_ready, c + 1)
                        score_vectors(c + 1)

            chunk(0, True, False)
            with pe.Fori(1, CHUNKS - 1) as c:
                chunk(c, False, False)
            chunk(CHUNKS - 1, False, True)
            transpose_ctx(CHUNKS - 1, R - 2, False)
            for odd in range(2):
                weighted(CHUNKS - 1, R - 1, odd, False)
            transpose_ctx(CHUNKS - 1, R - 1, False)
            pe.wait_ge(y_copied, CHUNKS - 1)
            project(CHUNKS - 1)


_INS = ["r_target_item", "r_history_sequence", "r_mask", "L0_rec_W_q", "L0_rec_W_k", "L0_rec_W_v", "L0_rec_W_o"]


def kernel(**inputs):
    import concourse.bacc as bacc
    import numpy as np
    from concourse.bass_utils import run_bass_kernel_spmd

    nc = bacc.Bacc("TRN2", target_bir_lowering=False, num_devices=1)
    arrays, args = {}, []
    for name in _INS:
        a = np.ascontiguousarray(inputs[name])
        arrays[name] = a
        args.append(nc.dram_tensor(name, a.shape, mybir.dt.from_np(a.dtype), kind="ExternalInput").ap())
    y = nc.dram_tensor("y", inputs["r_target_item"].shape, mybir.dt.float32, kind="ExternalOutput").ap()
    target_attention(nc, *args, y)
    return run_bass_kernel_spmd(nc, [arrays], core_ids=[0]).results[0]["y"]
```
